# Optimizing a Trainium2 kernel written in Bass

```python
import numpy as np
import jax
import jax.numpy as jnp

def _softmax(x, axis=-1):
    return jax.nn.softmax(x, axis=axis)

def _gelu(x):
    return jax.nn.gelu(x, approximate=True)

def _silu(x):
    return jax.nn.silu(x)

def _sigmoid(x):
    return jax.nn.sigmoid(x)

def _layernorm(x, axis=-1, eps=1e-05):
    m = jnp.mean(x, axis=axis, keepdims=True)
    v = jnp.var(x, axis=axis, keepdims=True)
    return (x - m) / jnp.sqrt(v + eps)

def _scatter_add(tgt, idx, src, axis=0):
    return tgt.at[idx].add(src)

def _segment_sum(src, seg, n):
    return jax.ops.segment_sum(src, seg, n)
kernel_name = 'mk_cond_resid_d1_seqx_r2_2180f5'

def setup_inputs(seed: int=0):
    np.random.seed(seed)
    _w = jnp.asarray

    def _rec_inputs():
        import jax
        import jax.numpy as jnp
        _rk = jax.random.key(seed)
        x = -7.109e-05 + 0.9999 * jax.random.normal(jax.random.fold_in(_rk, 1), (64, 128, 2048), jnp.float32)
        _lenS = 128 - jax.random.randint(jax.random.fold_in(_rk, 7), (64,), 0, max(1, 128 // 4) + 1, jnp.int32)
        _lenS2 = 128 - jax.random.randint(jax.random.fold_in(_rk, 8), (64,), 0, max(1, 128 // 4) + 1, jnp.int32)
        itok_B_0_15 = jax.random.randint(jax.random.fold_in(_rk, 11), (64,), 0, 16, jnp.int32)
        return (x, itok_B_0_15)
    x, itok_B_0_15 = _rec_inputs()

    def _L0_cond_setup():
        import jax, jax.numpy as jnp
        import numpy as np
        B, C, T = (64, 128, 2048)
        S, D = (16, 128)
        key = jax.random.key(seed)
        k1, k2, k3 = jax.random.split(key, 3)
        x = jax.random.normal(k1, (B, C, T), dtype=jnp.float32)
        condition = jax.random.randint(k2, (B,), 0, S, dtype=jnp.int64)
        bound = float(np.sqrt(6.0 / C))
        weights = jax.random.uniform(k3, (S, C, D), dtype=jnp.float32, minval=-bound, maxval=bound)
        return {'x': x, 'condition': condition, 'weights': weights}
    _L0_cond_all = _L0_cond_setup()
    _L0_cond_in = {k: v for k, v in _L0_cond_all.items() if k in ('weights',)}
    del _L0_cond_all
    return {'x': x, 'itok_B_0_15': itok_B_0_15, 'L0_cond_weights': _L0_cond_in['weights']}

def reference(x, itok_B_0_15, L0_cond_weights):
    import jax
    import jax.numpy as jnp

    def _L0_cond_ref(x, condition, weights):
        import jax, jax.numpy as jnp
        import numpy as np
        B, C, T = (64, 128, 2048)
        S, D = (16, 128)
        W = weights[condition]
        return jnp.einsum('bct,bcd->bdt', x, W)
    x = x + _L0_cond_ref(x, itok_B_0_15, L0_cond_weights)
    return x

_drawn_inputs = setup_inputs


def setup_inputs(seed=0):
    import zlib

    import numpy as np

    out = dict(_drawn_inputs(seed))
    spreads = {}
    factors = {}
    for name, (base, spread) in spreads.items():
        noise = np.random.default_rng([zlib.crc32(name.encode()), seed]).standard_normal(out[name].shape)
        drawn = base * np.exp(spread * noise) if base else spread * noise
        out[name] = jnp.asarray(drawn.astype(out[name].dtype))
    for name, factor in factors.items():
        out[name] = (out[name] * factor).astype(out[name].dtype)
    return out
```

```python
from contextlib import ExitStack

import concourse.bass as bass
from concourse import mybir
from concourse.alu_op_type import AluOpType

BANK_COLUMNS = 512
PSUM_BANKS = 8
STEPS = 4
RING_TURNS = 4


def conditioned_residual(nc, x, condition, weights, out):
    fp32 = mybir.dt.float32
    batches, channels, time = x.shape
    states, _, features = weights.shape
    turns = batches // STEPS
    matmuls = time // BANK_COLUMNS
    psum_slots = PSUM_BANKS // matmuls

    with ExitStack() as ctx:
        def sbuf(name, shape, dtype=fp32):
            return ctx.enter_context(nc.sbuf_tensor(name, shape, dtype))

        def sem(name):
            return ctx.enter_context(nc.semaphore(name))

        x_ring = sbuf("x_ring", [channels, RING_TURNS * STEPS * time])
        weight_table = sbuf("weight_table", [channels, states * features])
        chosen_weights = [sbuf(f"chosen_weights{u}", [channels, features]) for u in range(STEPS)]
        condition_row = sbuf("condition_row", [1, batches], condition.dtype)
        product = ctx.enter_context(nc.psum_tensor("product", [features, psum_slots, time], fp32))

        condition_loaded = sem("condition_loaded")
        table_loaded = sem("table_loaded")
        x_loaded = [sem(f"x_loaded{u}") for u in range(STEPS)]
        out_stored = [sem(f"out_stored{u}") for u in range(STEPS)]
        weights_chosen = sem("weights_chosen")
        product_done = sem("product_done")
        sum_done = sem("sum_done")

        def ring_column(turn, u):
            return (turn % RING_TURNS) * (STEPS * time) + u * time

        block = ctx.enter_context(nc.Block())

        @block.sync
        def _(sp):
            def load(turn, u):
                sp.dma_start(x_ring[:, bass.ds(ring_column(turn, u), time)],
                             x[bass.ds(turn * STEPS + u, 1)].rearrange("b c t -> c (b t)")
                             ).then_inc(x_loaded[u], 16)

            for u in range(STEPS):
                load(0, u)
            with sp.Fori(1, RING_TURNS) as turn:
                for u in range(STEPS):
                    sp.wait_ge(x_loaded[u], 16 * turn)
                    load(turn, u)
            with sp.Fori(RING_TURNS, turns) as turn:
                for u in range(STEPS):
                    sp.wait_ge(x_loaded[u], 16 * turn)
                    sp.wait_ge(out_stored[u], 16 * (turn - RING_TURNS + 1))
                    load(turn, u)

        @block.gpsimd
        def _(pool):
            def choose(turn, u):
                state = pool.value_load(condition_row[0:1, bass.ds(turn * STEPS + u, 1)],
                                        min_val=0, max_val=states - 1)
                pool.tensor_copy(chosen_weights[u][:, :],
                                 weight_table[:, bass.ds(state * features, features)]
                                 ).then_inc(weights_chosen, 1)

            pool.wait_ge(condition_loaded, 16)
            pool.wait_ge(table_loaded, 16)
            for u in range(STEPS):
                choose(0, u)
            with pool.Fori(1, turns) as turn:
                for u in range(STEPS):
                    pool.wait_ge(product_done, (turn - 1) * STEPS + u + 1)
                    choose(turn, u)

        @block.tensor
        def _(pe):
            def multiply(turn, u):
                pe.wait_ge(x_loaded[u], 16 * (turn + 1))
                pe.wait_ge(weights_chosen, turn * STEPS + u + 1)
                for m in range(matmuls):
                    last = pe.matmul(product[:, u % psum_slots, m * BANK_COLUMNS:(m + 1) * BANK_COLUMNS],
                                     chosen_weights[u][:, :],
                                     x_ring[:, bass.ds(ring_column(turn, u) + m * BANK_COLUMNS, BANK_COLUMNS)],
                                     start=True, stop=True)
                last.then_inc(product_done, 1)

            for u in range(STEPS):
                if u >= psum_slots:
                    pe.wait_ge(sum_done, u - psum_slots + 1)
                multiply(0, u)
            with pe.Fori(1, turns) as turn:
                for u in range(STEPS):
                    pe.wait_ge(sum_done, turn * STEPS + u - psum_slots + 1)
                    multiply(turn, u)

        @block.vector
        def _(dve):
            with dve.Fori(0, turns) as turn:
                for u in range(STEPS):
                    tile = x_ring[:, bass.ds(ring_column(turn, u), time)]
                    dve.wait_ge(product_done, turn * STEPS + u + 1)
                    dve.tensor_tensor(tile, product[:, u % psum_slots, :], tile,
                                      AluOpType.add).then_inc(sum_done, 1)

        @block.scalar
        def _(act):
            def store(turn, u):
                act.wait_ge(sum_done, turn * STEPS + u + 1)
                act.dma_start(out[bass.ds(turn * STEPS + u, 1)].rearrange("b c t -> c (b t)"),
                              x_ring[:, bass.ds(ring_column(turn, u), time)]
                              ).then_inc(out_stored[u], 16)

            act.dma_start(condition_row[0:1, :], condition.rearrange("(o b) -> o b", o=1)
                          ).then_inc(condition_loaded, 16)
            act.dma_start(weight_table[:, :].rearrange("c (s d) -> c s d", s=states),
                          weights.rearrange("s c d -> c s d")).then_inc(table_loaded, 16)
            for u in range(STEPS):
                store(0, u)
            with act.Fori(1, turns) as turn:
                for u in range(STEPS):
                    act.wait_ge(out_stored[u], 16 * turn)
                    store(turn, u)
            for u in range(STEPS):
                act.wait_ge(out_stored[u], 16 * turns)


def kernel(x, itok_B_0_15, L0_cond_weights):
    import numpy as np
    import concourse.bacc as bacc
    from concourse.bass_utils import run_bass_kernel_spmd

    nc = bacc.Bacc("TRN2", target_bir_lowering=False, num_devices=1)
    arrays = {
        "x": np.ascontiguousarray(x),
        "condition": np.ascontiguousarray(itok_B_0_15),
        "weights": np.ascontiguousarray(L0_cond_weights),
    }
    args = [nc.dram_tensor(name, a.shape, mybir.dt.from_np(a.dtype), kind="ExternalInput").ap()
            for name, a in arrays.items()]
    out = nc.dram_tensor("out", arrays["x"].shape, mybir.dt.float32, kind="ExternalOutput").ap()
    conditioned_residual(nc, *args, out)
    result = run_bass_kernel_spmd(nc, [arrays], core_ids=[0])
    return result.results[0]["out"]
```
